# Optimizing a Trainium2 kernel written in Bass

```python
import numpy as np
import jax
import jax.numpy as jnp

def _softmax(x, axis=-1):
    return jax.nn.softmax(x, axis=axis)

def _gelu(x):
    return jax.nn.gelu(x, approximate=True)

def _silu(x):
    return jax.nn.silu(x)

def _sigmoid(x):
    return jax.nn.sigmoid(x)

def _layernorm(x, axis=-1, eps=1e-05):
    m = jnp.mean(x, axis=axis, keepdims=True)
    v = jnp.var(x, axis=axis, keepdims=True)
    return (x - m) / jnp.sqrt(v + eps)

def _scatter_add(tgt, idx, src, axis=0):
    return tgt.at[idx].add(src)

def _segment_sum(src, seg, n):
    return jax.ops.segment_sum(src, seg, n)
kernel_name = 'mk_gnn_resnorm_d2_gnn_r8_54aa1e'

def setup_inputs(seed: int=0):
    np.random.seed(seed)
    _w = jnp.asarray

    def _rec_inputs():
        import jax
        import jax.numpy as jnp
        _gk = jax.random.key(seed)
        x = -0.0003713 + 1 * jax.random.normal(jax.random.fold_in(_gk, 1), (12500, 128), jnp.float32)
        src = jax.random.randint(jax.random.fold_in(_gk, 2), (200000,), 0, 12500, jnp.int32)
        dst = jnp.minimum((12500 * jax.random.uniform(jax.random.fold_in(_gk, 3), (200000,)) ** 2.0).astype(jnp.int32), 99999)
        _o = jnp.argsort(dst, stable=True)
        src = src[_o]
        dst = dst[_o]
        edge_type_8 = jax.random.randint(jax.random.fold_in(_gk, 12), (200000,), 0, 8, jnp.int32)
        return (x, src, dst, edge_type_8)
    x, src, dst, edge_type_8 = _rec_inputs()

    def _L0_gnn_setup():
        import jax, jax.numpy as jnp
        import numpy as np
        N_NODES = 12500
        N_EDGES = 400000
        D_IN = 128
        D_OUT = 128
        key = jax.random.key(seed)
        k1, k2, k3, k4 = jax.random.split(key, 4)
        x = jax.random.normal(k1, (N_NODES, D_IN), dtype=jnp.float32)
        edge_index = jax.random.randint(k2, (2, N_EDGES), 0, N_NODES, dtype=jnp.int32)
        W = jax.random.normal(k3, (D_OUT, D_IN), dtype=jnp.float32) * (1.0 / np.sqrt(D_IN))
        b = jax.random.normal(k4, (D_OUT,), dtype=jnp.float32) * 0.01
        return {'x': x, 'edge_index': edge_index, 'W': W, 'b': b}
    _L0_gnn_all = _L0_gnn_setup()
    _L0_gnn_in = {k: v for k, v in _L0_gnn_all.items() if k in ('W', 'b')}
    del _L0_gnn_all

    def _L1_gnn_setup():
        import jax, jax.numpy as jnp
        import numpy as np
        NUM_NODES = 6250
        NUM_EDGES = 200000
        DIM = 128
        NUM_REL = 8
        NUM_LAYERS = 2

        def _rgcn_conv(x, W, root, bias, src, dst, etype):
            R, N = (W.shape[0], x.shape[0])
            xW = jnp.einsum('ni,rio->rno', x, W)
            msgs = xW[etype, src]
            seg = etype * N + dst
            agg = jax.ops.segment_sum(msgs, seg, num_segments=R * N)
            cnt = jax.ops.segment_sum(jnp.ones_like(seg, dtype=x.dtype), seg, num_segments=R * N)
            agg = agg / jnp.maximum(cnt, 1.0)[:, None]
            agg = agg.reshape(R, N, -1).sum(axis=0)
            return agg + x @ root + bias
        key = jax.random.key(seed)
        ks = jax.random.split(key, 8)
        x = jax.random.normal(ks[0], (NUM_NODES, DIM), dtype=jnp.float32)
        edge_index = jax.random.randint(ks[1], (2, NUM_EDGES), 0, NUM_NODES, dtype=jnp.int32)
        edge_types = jax.random.randint(ks[2], (NUM_EDGES,), 0, NUM_REL, dtype=jnp.int32)
        scale = 1.0 / np.sqrt(DIM)
        weights = jax.random.normal(ks[3], (NUM_LAYERS, NUM_REL, DIM, DIM), dtype=jnp.float32) * scale
        roots = jax.random.normal(ks[4], (NUM_LAYERS, DIM, DIM), dtype=jnp.float32) * scale
        biases = jnp.zeros((NUM_LAYERS, DIM), dtype=jnp.float32)
        return {'x': x, 'weights': weights, 'roots': roots, 'biases': biases, 'edge_index': edge_index, 'edge_types': edge_types}
    _L1_gnn_all = _L1_gnn_setup()
    _L1_gnn_in = {k: v for k, v in _L1_gnn_all.items() if k in ('weights', 'roots', 'biases')}
    del _L1_gnn_all
    return {'x': x, 'src': src, 'dst': dst, 'edge_type_8': edge_type_8, 'L0_gnn_W': _L0_gnn_in['W'], 'L0_gnn_b': _L0_gnn_in['b'], 'L1_gnn_weights': _L1_gnn_in['weights'], 'L1_gnn_roots': _L1_gnn_in['roots'], 'L1_gnn_biases': _L1_gnn_in['biases']}

def reference(x, src, dst, edge_type_8, L0_gnn_W, L0_gnn_b, L1_gnn_weights, L1_gnn_roots, L1_gnn_biases):
    import jax
    import jax.numpy as jnp

    def _L0_gnn_ref(x, edge_index, W, b):
        import jax, jax.numpy as jnp
        import numpy as np
        N_NODES = 12500
        N_EDGES = 400000
        D_IN = 128
        D_OUT = 128
        row, col = (edge_index[0], edge_index[1])
        deg = jax.ops.segment_sum(jnp.ones(row.shape[0], dtype=x.dtype), row, num_segments=N_NODES)
        deg_inv_sqrt = jnp.where(deg > 0, jax.lax.rsqrt(deg), 0.0)
        norm = deg_inv_sqrt[row] * deg_inv_sqrt[col]
        xl = x @ W.T + b
        out = jax.ops.segment_sum(norm[:, None] * xl[col], row, num_segments=N_NODES)
        return out

    def _L1_gnn_ref(x, weights, roots, biases, edge_index, edge_types):
        import jax, jax.numpy as jnp
        import numpy as np
        NUM_NODES = 6250
        NUM_EDGES = 200000
        DIM = 128
        NUM_REL = 8
        NUM_LAYERS = 2

        def _rgcn_conv(x, W, root, bias, src, dst, etype):
            R, N = (W.shape[0], x.shape[0])
            xW = jnp.einsum('ni,rio->rno', x, W)
            msgs = xW[etype, src]
            seg = etype * N + dst
            agg = jax.ops.segment_sum(msgs, seg, num_segments=R * N)
            cnt = jax.ops.segment_sum(jnp.ones_like(seg, dtype=x.dtype), seg, num_segments=R * N)
            agg = agg / jnp.maximum(cnt, 1.0)[:, None]
            agg = agg.reshape(R, N, -1).sum(axis=0)
            return agg + x @ root + bias
        src, dst = (edge_index[0], edge_index[1])
        h = x
        for l in range(NUM_LAYERS - 1):
            h = _rgcn_conv(h, weights[l], roots[l], biases[l], src, dst, edge_types)
            h = jax.nn.relu(h)
        h = _rgcn_conv(h, weights[-1], roots[-1], biases[-1], src, dst, edge_types)
        return h
    edge_index = jnp.stack([src, dst])
    x = _layernorm(x + _L0_gnn_ref(x, edge_index, L0_gnn_W, L0_gnn_b), axis=-1)
    x = _layernorm(x + _L1_gnn_ref(x, L1_gnn_weights, L1_gnn_roots, L1_gnn_biases, edge_index, edge_type_8), axis=-1)
    return x

_drawn_inputs = setup_inputs


def setup_inputs(seed=0):
    import zlib

    import numpy as np

    out = dict(_drawn_inputs(seed))
    spreads = {'L1_gnn_biases': (0.0, 0.1)}
    factors = {'L0_gnn_b': 3.85}
    for name, (base, spread) in spreads.items():
        noise = np.random.default_rng([zlib.crc32(name.encode()), seed]).standard_normal(out[name].shape)
        drawn = base * np.exp(spread * noise) if base else spread * noise
        out[name] = jnp.asarray(drawn.astype(out[name].dtype))
    for name, factor in factors.items():
        out[name] = (out[name] * factor).astype(out[name].dtype)
    return out
```

```python
from contextlib import ExitStack

import numpy as np

import concourse.bass as bass
from concourse import mybir

F32, BF16 = mybir.dt.float32, mybir.dt.bfloat16
I32, U32 = mybir.dt.int32, mybir.dt.uint32
ALU, ACT, AX = mybir.AluOpType, mybir.ActivationFunctionType, mybir.AxisListType

P = 128
D = 128
RELS = 8
K = 4
C = 4
EPS = 1e-5


class Count:

    def __init__(self, eng, sem):
        self.eng, self.sem, self.at = eng, sem, 0

    def link(self, ins):
        ins.then_inc(self.sem, 1)
        self.at = self.at + 1
        self.eng.wait_ge(self.sem, self.at)
        return ins


def loop(eng, n, body, count=None):
    base = count.at if count else 0
    body(0)
    step = count.at - base if count else 0
    with eng.Fori(1, n) as i:
        if count:
            count.at = base + i * step
        body(i)
    if count:
        count.at = base + n * step


def wait(eng, sem, value):
    if not isinstance(value, int) or value > 0:
        eng.wait_ge(sem, value)


def build(nc, x, src, dst, etype, W0, b0, weights, roots, biases, out):
    N, E = x.shape[0], src.shape[0]
    NT = -(-N // P)
    NP = NT * P
    TAIL = N - (NT - 1) * P
    QUAD = K * P
    IT = -(-E // (C * QUAD))
    ROWE = C * QUAD
    TPI = C * K
    ET = IT * TPI
    EP = IT * ROWE
    FULL, REST = E // ROWE, E % ROWE
    NB = NT + 1
    REC = D + 1
    HG = 14
    HT = ET // (2 * HG)
    XT = NT // HG
    assert IT == NT and ET == 2 * HG * HT and NT == HG * XT and NB <= P
    MAIN = RELS * D

    perm = nc.dram_tensor("permuted", [EP, REC], F32)
    table = nc.dram_tensor("table", [RELS * NP, D], F32)

    with ExitStack() as ctx:
        def sb(name, shape, dt):
            return ctx.enter_context(nc.sbuf_tensor(name, shape, dt))

        def psum(name, shape):
            return ctx.enter_context(nc.psum_tensor(name, shape, F32))

        def sem(name):
            return ctx.enter_context(nc.semaphore(name))

        xy = sb("xy", [P, NT, D], F32)
        acc_space = sb("acc_space", [P, NT * D + 176], F32)
        acc = acc_space[:, 0:NT * D].rearrange("p (t f) -> p t f", f=D)
        nat = acc_space[:, 0:3 * ROWE].bitcast(I32).rearrange("p (a e) -> p a e", a=3)
        natf = acc_space[:, 3 * ROWE:6 * ROWE].rearrange("p (a e) -> p a e", a=3)
        ohspace = acc_space[:, :].bitcast(BF16)
        HA = 2 * HT * NB
        hist_a = ohspace[:, 0:HA].rearrange("p (u t a) -> p u t a", u=2, a=NB)
        hist_b = ohspace[:, HA:HA + 2 * HT * P].rearrange("p (u t b) -> p u t b", u=2, b=P)
        src_c = sb("src_c", [P, ET], F32)
        dst_c = sb("dst_c", [P, ET], F32)
        idx_c = sb("idx_c", [P, ET], F32)
        w_c = sb("w_c", [P, ET], F32)
        et_c = sb("et_c", [P, ET], BF16)
        srct_c = sb("srct_c", [P, ET], BF16)
        srcl_c = sb("srcl_c", [P, ET], BF16)
        dstt_r = sb("dstt_r", [P, ROWE], BF16)
        dstl_r = sb("dstl_r", [P, ROWE], BF16)
        cnt = sb("cnt", [P, NT, RELS], F32)
        rec = sb("rec", [P, C, K, REC], F32)
        msg = rec[:, :, :, :].rearrange("p c k f -> p c (k f)")[:, :, 0:K * D].rearrange(
            "p c (k f) -> p c k f", k=K)
        slot_u = sb("slot_u", [P, C, K], U32)
        ohT = sb("ohT", [P, 2, QUAD], F32)
        ohTx = sb("ohTx", [P, QUAD], F32)
        ohN = sb("ohN", [P, 2, K, P], F32)
        ohNx = sb("ohNx", [P, K, P], F32)
        ohA = sb("ohA", [P, 2, K + 1, NB], BF16)
        ohD = sb("ohD", [P, 2, K, P], BF16)
        ohDx = sb("ohDx", [P, K, P], BF16)
        ohR = sb("ohR", [P, 2, K, RELS], BF16)
        rel = sb("rel", [P, 2, K], F32)
        relx = sb("relx", [P, K], F32)
        rank_t = sb("rank_t", [P, K, NB], F32)
        run = sb("run", [P, NB], F32)
        wprod = sb("wprod", [P, K, RELS], F32)
        w_all = sb("w_all", [P, (RELS + 1) * D], F32)
        stage = rec[:, :, :, :].rearrange("p c k f -> p (c k f)")[:, 0:2 * MAIN].rearrange(
            "p (b m) -> p b m", b=2)
        h_in = stage[:, 0, 0:XT * D].rearrange("p (k f) -> p k f", f=D)
        h_tr = stage[:, 1, 0:XT * D].rearrange("p (k f) -> p k f", f=D)
        hs = sb("hs", [P, 2, D], F32)
        hT = sb("hT", [P, 2, D], F32)
        w0 = sb("w0", [P, D], F32)
        w0T = sb("w0T", [P, D], F32)
        b_row = sb("b_row", [1, D], F32)
        bias_row = sb("bias_row", [1, 2 * D], F32)
        bias_all = sb("bias_all", [P, 2, D], F32)
        ident = sb("ident", [P, P], F32)
        ident_b = sb("ident_b", [P, P], BF16)
        ident_s = sb("ident_s", [P, P], BF16)
        before = sb("before", [P, P], F32)
        before_b = sb("before_b", [P, P], BF16)
        ones = sb("ones", [P, P], F32)
        ones_b = sb("ones_b", [P, P], BF16)
        zeros_b = sb("zeros_b", [1, QUAD], BF16)
        iota_r = sb("iota_r", [P, P], F32)
        iota_b = sb("iota_b", [P, P], BF16)
        iota_p = sb("iota_p", [P, NT], F32)
        off = sb("off", [P, NT], F32)
        posq = sb("posq", [P, 2 * C], F32)
        small_i = sb("small_i", [P, 2 * C], I32)
        tab_n = sb("tab_n", [P, 3 * C], F32)
        tab_s = sb("tab_s", [P, 3 * C], F32)
        tdiff = sb("tdiff", [P, C], F32)
        tscan = sb("tscan", [P, C], F32)
        tbase = sb("tbase", [P, 1], F32)
        row_n = sb("row_n", [1, 3 * C, IT], I32)
        row_s = sb("row_s", [1, 3 * C, IT], I32)
        junk = sb("junk", [P, NT], F32)
        deg = sb("deg", [P, NB], F32)
        dis = sb("dis", [P, NT], F32)
        dtmp = sb("dtmp", [P, NT], F32)
        tot = sb("tot", [P, 1], F32)
        starts = sb("starts", [P, NB], F32)
        stats = sb("stats", [P, NT, 6], F32)
        mean = sb("mean", [P, NT], F32)
        rstd = sb("rstd", [P, NT], F32)
        half = sb("half", [P, NT], F32)
        eps_t = sb("eps_t", [P, 1], F32)

        pB, pR, pY0, pY1, pC, pX, pT0, pT1 = (psum(n, [P, 512]) for n in
                                              ("pB", "pR", "pY0", "pY1", "pC", "pX", "pT0", "pT1"))
        pY, pT = (pY0, pY1), (pT0, pT1)

        s_pads, s_iota, s_edges, s_x, s_w = (sem(n) for n in ("pads", "iotas", "edges_in", "x_in", "w_in"))
        s_rows_f, s_cols_ps, s_cols = sem("rows_f32"), sem("cols_in_psum"), sem("cols_copied")
        s_dve0, s_consts = sem("dve_setup"), sem("consts")
        s_tab, s_tab_ps, s_wt, s_wt_c = sem("tab"), sem("tab_in_psum"), sem("w0T_in_psum"), sem("w0T_copied")
        NG = 3 * TPI // 4

        def range_table(eng, count, tab, s_ready, s_back, at):
            count.link(eng.tensor_scalar(tab[:, 0:2 * C], tab[:, 0:2 * C], float(NT - 1), None, ALU.min))
            count.link(eng.tensor_tensor(tdiff[:, :], tab[:, C:2 * C], tab[:, 0:C], ALU.subtract))
            eng.sem_inc(s_ready, 1)
            eng.wait_ge(s_back, at)
            count.link(eng.tensor_reduce(tbase[:, :], pC[:, 0:C], AX.X, ALU.add))
            count.link(eng.tensor_tensor_scan(tscan[:, :], ones[:, 0:C], tdiff[:, :], tbase[:, 0:1],
                                              ALU.mult, ALU.add))
            count.link(eng.tensor_tensor(tab[:, 2 * C:3 * C], tscan[:, :], tdiff[:, :], ALU.subtract))
            eng.sem_inc(s_ready, 1)

        def range_products(eng, tab, s_ready, s_back, ready0, banks):
            eng.wait_ge(s_ready, ready0 + 1)
            eng.matmul(pC[:, 0:C], before[:, :], tdiff[:, :], start=True, stop=True).then_inc(s_back, 1)
            eng.wait_ge(s_ready, ready0 + 2)
            for j in range(3 * C):
                mm = eng.matmul(banks[j // C][0:1, (j % C) * IT:(j % C + 1) * IT], tab[:, j:j + 1],
                                ident[:, 0:IT], start=True, stop=True)
            mm.then_inc(s_back, 1)

        with nc.Block() as block:
            @block.sync
            def _(sp):
                sp.wait_ge(s_pads, 1)
                for a, arr in enumerate((src, dst, etype)):
                    sp.dma_start(nat[0:FULL, a, :], arr[0:FULL * ROWE].rearrange("(i e) -> i e", e=ROWE)
                                 ).then_inc(s_edges, 16)
                    sp.dma_start(nat[FULL:FULL + 1, a, 0:REST],
                                 arr[FULL * ROWE:E].rearrange("(i e) -> i e", i=1)).then_inc(s_edges, 16)
                sp.dma_start(w0[:, :], W0).then_inc(s_w, 16)
                sp.dma_start(b_row[:, :], b0.rearrange("(a f) -> a f", a=1)).then_inc(s_w, 16)
                sp.dma_start(bias_row[:, :], biases.rearrange("(a l) f -> a (l f)", a=1)).then_inc(s_w, 16)
                sp.dma_start(w_all[:, 0:MAIN].rearrange("p (r o) -> p r o", r=RELS),
                             weights[0].rearrange("r i o -> i r o")).then_inc(s_w, 16)
                sp.dma_start(w_all[:, MAIN:MAIN + D], roots[0]).then_inc(s_w, 16)
                sp.wait_ge(s_pads, 2)
                sp.dma_start(xy[:, 0:NT - 1, :], x[0:(NT - 1) * P, :].rearrange("(t p) f -> p t f", p=P)
                             ).then_inc(s_x, 16)
                sp.dma_start(xy[0:TAIL, NT - 1, :], x[(NT - 1) * P:N, :]).then_inc(s_x, 16)

            @block.gpsimd
            def _(pool):
                pool.memset(nat[:, 0:2, :], NP)
                pool.memset(nat[:, 2, :], 0).then_inc(s_pads, 1)
                pool.memset(xy[:, NT - 1, :], 0.0).then_inc(s_pads, 1)
                kw = dict(allow_small_or_imprecise_dtypes=True)
                pool.iota(iota_r[:, :], [[1, P]], base=0, channel_multiplier=0, **kw)
                pool.iota(iota_p[:, :], [[P, NT]], base=0, channel_multiplier=1, **kw)
                pool.iota(off[:, :], [[P, NT]], base=0, channel_multiplier=0, **kw)
                pool.iota(posq[:, :].rearrange("p (e c) -> p e c", e=2), [[QUAD - 1, 2], [QUAD, C]],
                          base=0, channel_multiplier=ROWE, **kw).then_inc(s_iota, 1)

            @block.vector
            def _(dve):
                n = Count(dve, s_dve0)
                dve.memset(ones[:, :], 1.0)
                dve.memset(ones_b[:, :], 1.0)
                dve.memset(zeros_b[:, :], 0.0)
                dve.memset(ohA[:, :, K, :], 0.0)
                dve.memset(tot[:, :], 0.0)
                dve.memset(eps_t[:, :], EPS)
                dve.memset(cnt[:, :, :], 0.0)
                dve.wait_ge(s_iota, 1)
                dve.tensor_copy(iota_b[:, :], iota_r[:, :])
                n.link(dve.tensor_scalar(ident[:, :], iota_r[:, :], iota_p[:, 0:1], None, ALU.is_equal))
                dve.tensor_copy(ident_b[:, :], ident[:, :])
                dve.tensor_scalar(ident_s[:, :], ident[:, :], float(P), None, ALU.mult)
                n.link(dve.tensor_scalar(before[:, :], iota_r[:, :], iota_p[:, 0:1], None, ALU.is_gt))
                dve.tensor_copy(before_b[:, :], before[:, :]).then_inc(s_consts, 1)
                dve.wait_ge(s_edges, 96)
                n.link(dve.tensor_copy(natf, nat))
                dve.sem_inc(s_rows_f, 1)
                n.link(dve.tensor_scalar(nat[:, 0, :], nat[:, 1, :], 7, None, ALU.arith_shift_right))
                n.link(dve.tensor_copy(dstt_r[:, :], nat[:, 0, :]))
                n.link(dve.tensor_scalar(nat[:, 0, :], nat[:, 1, :], P - 1, None, ALU.bitwise_and))
                n.link(dve.tensor_copy(dstl_r[:, :], nat[:, 0, :]))
                quads = natf[:, 1, :].rearrange("p (c e) -> p c e", c=C)
                n.link(dve.tensor_reduce(tab_n[:, 0:C], quads, AX.X, ALU.min))
                n.link(dve.tensor_reduce(tab_n[:, C:2 * C], quads, AX.X, ALU.max))
                n.link(dve.tensor_copy(small_i[:, :], tab_n[:, 0:2 * C]))
                n.link(dve.tensor_scalar(small_i[:, :], small_i[:, :], 7, None, ALU.arith_shift_right))
                n.link(dve.tensor_copy(tab_n[:, 0:2 * C], small_i[:, :]))
                range_table(dve, n, tab_n, s_tab, s_tab_ps, 1)
                dve.wait_ge(s_tab_ps, 2)
                for m, bank in enumerate((pB, pR, pX)):
                    dve.tensor_copy(row_n[0:1, m * C:(m + 1) * C, :],
                                    bank[0:1, 0:C * IT].rearrange("p (c i) -> p c i", c=C))
                dve.wait_ge(s_tab_ps, 3)
                dve.tensor_copy(bias_all[:, :, :], pC[:, 256:512].rearrange("p (l f) -> p l f", l=2))
                dve.wait_ge(s_cols, NG)
                dve.tensor_copy(et_c[:, :], w_c[:, :])
                dve.scalar_tensor_tensor(out=idx_c[:, :], in0=w_c[:, :], scalar=float(NP), in1=src_c[:, :],
                                         op0=ALU.mult, op1=ALU.add)
                ints = nat[:, 1, 0:ET]
                ints2 = nat[:, 2, 0:ET]
                n.link(dve.tensor_copy(ints, src_c[:, :]))
                n.link(dve.tensor_scalar(ints2, ints, 7, None, ALU.arith_shift_right))
                n.link(dve.tensor_copy(srct_c[:, :], ints2))
                n.link(dve.tensor_scalar(ints2, ints, P - 1, None, ALU.bitwise_and))
                n.link(dve.tensor_copy(srcl_c[:, :], ints2))

            @block.tensor
            def _(pe):
                pe.wait_ge(s_consts, 1)
                pe.wait_ge(s_w, 80)
                pe.transpose(pY0[:, 0:D], w0[:, :], ident[:, :]).then_inc(s_wt, 1)
                pe.wait_ge(s_rows_f, 1)
                for g in range(NG):
                    if g >= 2:
                        pe.wait_ge(s_cols, g - 1)
                    for k in range(4):
                        a, j = divmod(4 * g + k, TPI)
                        mm = pe.transpose(pT[g % 2][:, k * P:(k + 1) * P], natf[:, a, j * P:(j + 1) * P],
                                          ident[:, :])
                    mm.then_inc(s_cols_ps, 1)
                range_products(pe, tab_n, s_tab, s_tab_ps, 0, (pB, pR, pX))
                pe.matmul(pC[:, 256:512], ones[0:1, :], bias_row[:, :], start=True, stop=True
                          ).then_inc(s_tab_ps, 1)

            @block.scalar
            def _(act):
                act.wait_ge(s_wt, 1)
                act.copy(w0T[:, :], pY0[:, 0:D]).then_inc(s_wt_c, 1)
                for g in range(NG):
                    a, j = divmod(4 * g, TPI)
                    col = (src_c, dst_c, w_c)[a][:, :].rearrange("p (i j) -> p j i", j=TPI)[:, j:j + 4, :]
                    act.wait_ge(s_cols_ps, g + 1)
                    act.copy(col, pT[g % 2][:, :].rearrange("p (k i) -> p k i", k=4)[:, :, 0:IT]
                             ).then_inc(s_cols, 1)

        s_ha, s_hused = [sem("hist_onehot0"), sem("hist_onehot1")], [sem("hist_used0"), sem("hist_used1")]
        s_xc, s_xt, s_xtc, s_xm, s_xo = (sem(n) for n in ("x_copied", "x_transposed", "xT_copied", "xl_made", "xl_out"))
        s_dve1, s_deg, s_deg_c, s_tot, s_tot_c, s_st = (sem(n) for n in (
            "dve_hist", "deg_summed", "deg_copied", "totals", "totals_copied", "starts_made"))
        s_stab, s_stab_ps, s_sq, s_sqd = sem("stab"), sem("stab_in_psum"), sem("deg_clamped"), sem("deg_rooted")

        s_act_turn, s_pool_turn, s_dve_turn = sem("act_turn"), sem("pool_turn"), sem("dve_turn")

        with nc.Block() as block:
            @block.vector
            def _(dve):
                n = Count(dve, s_dve1)

                def body(i):
                    for u in range(2):
                        wait(dve, s_hused[u], i)
                        at = i * (2 * HT) + u * HT
                        dve.tensor_tensor(
                            hist_a[:, u], iota_b[:, 0:NB].unsqueeze(1).broadcast_to([P, HT, NB]),
                            srct_c[:, bass.ds(at, HT)].unsqueeze(2).broadcast_to([P, HT, NB]), ALU.is_equal)
                        dve.tensor_tensor(
                            hist_b[:, u], iota_b[:, :].unsqueeze(1).broadcast_to([P, HT, P]),
                            srcl_c[:, bass.ds(at, HT)].unsqueeze(2).broadcast_to([P, HT, P]), ALU.is_equal
                        ).then_inc(s_ha[u], 1)

                loop(dve, HG, body)
                dve.wait_ge(s_deg, 1)
                dve.tensor_copy(deg[:, :], pC[:, 0:NB]).then_inc(s_deg_c, 1)
                dve.wait_ge(s_deg_c, 1)
                n.link(dve.tensor_scalar(dtmp[:, :], deg[:, 0:NT], 1.0, None, ALU.max))
                dve.sem_inc(s_sq, 1)
                dve.wait_ge(s_tot, 1)
                dve.tensor_copy(tot[0:NB, :], pB[0:NB, 0:1]).then_inc(s_tot_c, 1)
                dve.wait_ge(s_st, 1)
                n.link(dve.tensor_copy(starts[:, :], pR[:, 0:NB]))
                dve.tensor_copy(run[:, :], starts[:, :])
                for j in range(2 * C):
                    n.link(dve.tensor_scalar(junk[:, :], starts[:, 1:NB], posq[:, j:j + 1], 0.0,
                                             ALU.is_le, ALU.add, accum_out=tab_s[:, j:j + 1]))
                range_table(dve, n, tab_s, s_stab, s_stab_ps, 1)
                dve.wait_ge(s_stab_ps, 2)
                for m, bank in enumerate((pB, pX, pT0)):
                    dve.tensor_copy(row_s[0:1, m * C:(m + 1) * C, :],
                                    bank[0:1, 0:C * IT].rearrange("p (c i) -> p c i", c=C))
                dve.wait_ge(s_sqd, 1)
                n.link(dve.reciprocal(dis[:, :], dis[:, :]))
                n.link(dve.tensor_scalar(dtmp[:, :], deg[:, 0:NT], 1.0, None, ALU.min))
                n.link(dve.tensor_tensor(dis[:, :], dis[:, :], dtmp[:, :], ALU.mult))
                dve.wait_ge(s_xo, NT)
                dve.tensor_tensor(xy[:, :, :], xy[:, :, :],
                                  dis[:, :].unsqueeze(2).broadcast_to([P, NT, D]), ALU.mult)

            @block.tensor
            def _(pe):
                def body(i):
                    for k in range(XT):
                        pe.wait_ge(s_xc, i * XT + k + 1)
                        pe.transpose(pT[k // 4][:, k % 4 * P:(k % 4 + 1) * P], h_in[:, k, :], ident[:, :]
                                     ).then_inc(s_xt, 1)
                    for k in range(XT):
                        pe.wait_ge(s_xtc, i * XT + k + 1)
                        o = pY[k // 4][:, k % 4 * D:(k % 4 + 1) * D]
                        pe.matmul(o, ones[0:1, :], b_row[:, :], start=True, stop=False)
                        pe.matmul(o, h_tr[:, k, :], w0T[:, :], start=False, stop=True).then_inc(s_xm, 1)
                    for u in range(2):
                        pe.wait_ge(s_ha[u], i + 1)
                        for t in range(HT):
                            mm = pe.matmul(pC[:, 0:NB], hist_b[:, u, t, :], hist_a[:, u, t, :],
                                           start=isinstance(i, int) and u + t == 0, stop=False,
                                           skip_group_check=True)
                        mm.then_inc(s_hused[u], 1)

                pe.wait_ge(s_wt_c, 1)
                loop(pe, HG, body)
                pe.matmul(pC[:, 0:NB], zeros_b[:, 0:P], zeros_b[:, 0:NB], start=False, stop=True,
                          skip_group_check=True).then_inc(s_deg, 1)
                pe.wait_ge(s_deg_c, 1)
                pe.matmul(pB[0:NB, 0:1], deg[:, :], ones[:, 0:1], start=True, stop=True).then_inc(s_tot, 1)
                pe.wait_ge(s_tot_c, 1)
                pe.matmul(pR[:, 0:NB], tot[:, 0:1].broadcast_to([P, P]), before[:, 0:NB],
                          start=True, stop=True).then_inc(s_st, 1)
                range_products(pe, tab_s, s_stab, s_stab_ps, 0, (pB, pX, pT0))

            @block.scalar
            def _(act):
                def body(i):
                    for k in range(XT):
                        wait(act, s_xt, i * XT)
                        act.copy(h_in[:, k, :], xy[:, i * XT + k, :] if isinstance(i, int) else
                                 xy[:, bass.ds(i * XT + k, 1), :].rearrange("p a f -> p (a f)")
                                 ).then_inc(s_xc, 1)
                    for k in range(XT):
                        act.wait_ge(s_xt, i * XT + XT)
                        wait(act, s_xm, i * XT)
                        act.copy(h_tr[:, k, :], pT[k // 4][:, k % 4 * P:(k % 4 + 1) * P]).then_inc(s_xtc, 1)
                    act.wait_ge(s_xm, i * XT + XT)
                    act.sem_inc(s_act_turn, 1)
                    for k in range(XT):
                        act.copy(xy[:, bass.ds(i * XT + k, 1), :].rearrange("p a f -> p (a f)"),
                                 pY[k // 4][:, k % 4 * D:(k % 4 + 1) * D]).then_inc(s_xo, 1)

                act.wait_ge(s_x, 32)
                loop(act, HG, body)
                act.wait_ge(s_sq, 1)
                act.activation(dis[:, :], dtmp[:, :], ACT.Sqrt).then_inc(s_sqd, 1)


        def tile(t, i):
            return t[:, bass.ds(i, 1), :].rearrange("p a f -> p (a f)")

        def cols(t, i, c):
            return t[:, bass.ds(i * TPI + c * K, K)]

        def onehot_of(iota, columns, width):
            return (iota[:, 0:width].unsqueeze(1).broadcast_to([P, K, width]),
                    columns.unsqueeze(2).broadcast_to([P, K, width]))

        def span(eng, rows, i, c):
            lo = eng.value_load(rows[0:1, c, bass.ds(i, 1)], min_val=0, max_val=NT - 1)
            hi = eng.value_load(rows[0:1, C + c, bass.ds(i, 1)], min_val=0, max_val=NT - 1)
            return lo, hi

        def extras(eng, rows, i, c, lo, hi, body):
            with eng.If(lo < hi):
                first = eng.value_load(rows[0:1, 2 * C + c, bass.ds(i, 1)], min_val=0, max_val=IT * C * NT)
                with eng.Fori(first, first + hi - lo) as step:
                    body(nc.s_assert_within(step - first + lo + 1, 0, NT - 1), step)

        def spread_dst(pe, i, c, s_free, free, s_ready):
            wait(pe, s_free, free)
            es = slice(c * QUAD, (c + 1) * QUAD)
            pe.matmul(pB[:, :], ident_s[:, bass.ds(i, 1)].broadcast_to([P, P]), dstt_r[:, es],
                      start=True, stop=False)
            pe.matmul(pB[:, :], ident_b[:, bass.ds(i, 1)].broadcast_to([P, P]), dstl_r[:, es],
                      start=False, stop=True).then_inc(s_ready, 1)

        s_bc, s_ohT, s_ohA, s_rank, s_ohD, s_cps, s_yps, s_rec, s_pos, s_cadd = (sem(n) for n in (
            "dst_spread", "ohT_ready", "ohA_ready", "ranked", "ohD_ready", "counted", "y_picked",
            "rec_ready", "places_ready", "count_added"))
        s_scat = [sem(f"scattered{c}") for c in range(C)]
        s_dve2, s_xrel, s_xoh, s_xmm, s_xadd = (sem(n) for n in (
            "dve_permute", "extra_rel", "extra_onehots", "extra_products", "extra_added"))

        with nc.Block() as block:
            @block.vector
            def _(dve):
                n = Count(dve, s_dve2)

                def body(i):
                    for c in range(C):
                        q, b = i * C + c, c % 2
                        lo, hi = span(dve, row_n, i, c)
                        wait(dve, s_rank, q - 1)
                        dve.tensor_tensor(ohA[:, b, 0:K, :], *onehot_of(iota_b, cols(srct_c, i, c), NB),
                                          ALU.is_equal).then_inc(s_ohA, 1)
                        wait(dve, s_cps, q - 1)
                        dve.tensor_tensor(ohR[:, b], *onehot_of(iota_b, cols(et_c, i, c), RELS), ALU.is_equal)
                        n.link(dve.tensor_scalar(rel[:, b, :], cols(dst_c, i, c), off[:, bass.ds(lo, 1)], None,
                                                 ALU.subtract))
                        for k in range(K):
                            last = dve.tensor_scalar(ohD[:, b, k, :], iota_b[:, :], rel[:, b, k:k + 1], None,
                                                     ALU.is_equal)
                        last.then_inc(s_ohD, 1)
                        dve.wait_ge(s_bc, q + 1)

                        def extra(t, step):
                            dve.tensor_scalar(relx[:, :], cols(dst_c, i, c), off[:, bass.ds(t, 1)], None,
                                              ALU.subtract).then_inc(s_xrel, 1)
                            dve.tensor_scalar(ohTx[:, :], pB[:, :], iota_p[:, bass.ds(t, 1)], None, ALU.is_equal)
                            dve.wait_ge(s_xrel, step + 1)
                            for k in range(K):
                                last = dve.tensor_scalar(ohDx[:, k, :], iota_b[:, :], relx[:, k:k + 1], None,
                                                         ALU.is_equal)
                            last.then_inc(s_xoh, 1)
                            dve.wait_ge(s_xmm, step + 1)
                            wait(dve, s_cadd, q)
                            dve.tensor_tensor(tile(cnt, t), tile(cnt, t), pX[:, 0:RELS], ALU.add
                                              ).then_inc(s_xadd, 1)
                            dve.wait_ge(s_xadd, step + 1)
                            dve.sem_inc(s_dve_turn, 1)

                        dve.sem_inc(s_dve_turn, 1)
                        extras(dve, row_n, i, c, lo, hi, extra)
                        wait(dve, s_yps, q - 1)
                        dve.tensor_scalar(ohT[:, b, :], pB[:, :], iota_p[:, bass.ds(lo, 1)], None, ALU.is_equal
                                          ).then_inc(s_ohT, 1)
                        dve.wait_ge(s_rank, q + 1)
                        n.link(dve.tensor_tensor(
                            rank_t[:, :, :], pR[:, 0:K * NB].rearrange("p (k a) -> p k a", k=K),
                            run[:, :].unsqueeze(1).broadcast_to([P, K, NB]), ALU.add))
                        dve.tensor_tensor(run[:, :], run[:, :], pR[:, K * NB:(K + 1) * NB], ALU.add)
                        n.link(dve.tensor_tensor(rank_t[:, :, :], rank_t[:, :, :], ohA[:, b, 0:K, :], ALU.mult))
                        wait(dve, s_scat[c], i * 16 * K)
                        with nc.allow_low_precision(reason="whole numbers below 2^24, summed in float32"):
                            dve.tensor_reduce(slot_u[:, c, :], rank_t[:, :, :], AX.X, ALU.add).then_inc(s_pos, 1)
                        dve.wait_ge(s_cps, q + 1)
                        wait(dve, s_cadd, q)
                        dve.tensor_tensor(tile(cnt, lo), tile(cnt, lo), pC[:, 0:RELS], ALU.add
                                          ).then_inc(s_cadd, 1)

                loop(dve, IT, body, n)

            @block.tensor
            def _(pe):
                def body(i):
                    for c in range(C):
                        q, b = i * C + c, c % 2
                        lo, hi = span(pe, row_n, i, c)
                        spread_dst(pe, i, c, s_ohT, q, s_bc)
                        pe.wait_ge(s_ohA, q + 1)
                        wait(pe, s_pos, q)
                        pe.matmul(pR[:, 0:(K + 1) * NB], before_b[:, :], ohA[:, b, :, :], start=True, stop=False,
                                  skip_group_check=True)
                        for k in range(K):
                            last = pe.matmul(pR[:, (k + 1) * NB:(K + 1) * NB], ones_b[:, :],
                                             ohA[:, b, k:k + 1, :].broadcast_to([P, K - k, NB]),
                                             start=False, stop=k == K - 1, skip_group_check=True)
                        last.then_inc(s_rank, 1)
                        wait(pe, s_rec, 2 * (q - 1))
                        wait(pe, s_cadd, q)
                        pe.matmul(pY[b][:, :], zeros_b[:, 0:P], zeros_b[:, :], start=True, stop=False,
                                  skip_group_check=True)

                        def extra(t, step):
                            pe.wait_ge(s_xoh, step + 1)
                            for k in range(K):
                                pe.matmul(pY[b][:, k * D:(k + 1) * D], ohTx[:, k * P:(k + 1) * P], tile(xy, t),
                                          start=False, stop=False, skip_group_check=True)
                            for k in range(K):
                                last = pe.matmul(pX[:, 0:RELS], ohDx[:, k, :], ohR[:, b, k, :],
                                                 start=k == 0, stop=k == K - 1)
                            last.then_inc(s_xmm, 1)

                        extras(pe, row_n, i, c, lo, hi, extra)
                        pe.wait_ge(s_ohT, q + 1)
                        for k in range(K):
                            last = pe.matmul(pY[b][:, k * D:(k + 1) * D], ohT[:, b, k * P:(k + 1) * P], tile(xy, lo),
                                             start=False, stop=True, skip_group_check=True)
                        last.then_inc(s_yps, 1)
                        pe.wait_ge(s_ohD, q + 1)
                        for k in range(K):
                            last = pe.matmul(pC[:, 0:RELS], ohD[:, b, k, :], ohR[:, b, k, :],
                                             start=k == 0, stop=k == K - 1)
                        last.then_inc(s_cps, 1)

                loop(pe, IT, body)

            @block.scalar
            def _(act):
                def body(i):
                    for c in range(C):
                        q, b = i * C + c, c % 2
                        wait(act, s_scat[c], i * 16 * K)
                        act.wait_ge(s_yps, q + 1)
                        act.copy(rec[:, c, :, 0:D], pY[b][:, :].rearrange("p (k f) -> p k f", k=K)
                                 ).then_inc(s_rec, 1)
                        act.copy(rec[:, c, :, D:REC].rearrange("p k a -> p (k a)"), cols(src_c, i, c)
                                 ).then_inc(s_rec, 1)

                loop(act, IT, body)

            @block.gpsimd
            def _(pool):
                def body(i):
                    for c in range(C):
                        q = i * C + c
                        pool.wait_ge(s_rec, 2 * (q + 1))
                        pool.wait_ge(s_pos, q + 1)
                        pool.sem_inc(s_pool_turn, 1)
                        for k in range(K):
                            pool.indirect_dma_start(
                                perm[:, :], bass.IndirectOffsetOnAxis(ap=slot_u[:, c, k:k + 1], axis=0),
                                rec[:, c, k, :], None).then_inc(s_scat[c], 16)

                loop(pool, IT, body)
                for c in range(C):
                    pool.wait_ge(s_scat[c], IT * 16 * K)

        def reduce_pass(name, rows, gathered, weigh):
            s_in = [sem(f"{name}_rows_in{c}") for c in range(C)]
            (s_slot, s_oh, s_sum, s_add, s_dve, s_xrel, s_xoh, s_xmm, s_xadd) = (sem(f"{name}_{n}") for n in (
                "slot_ready", "onehots", "summed", "added", "dve", "extra_rel", "extra_onehots",
                "extra_summed", "extra_added"))
            if weigh:
                s_bc, s_ohT, s_wps, s_wok, s_wxoh, s_wxmm = (sem(f"{name}_{n}") for n in (
                    "dst_spread", "ohT_ready", "w_picked", "w_ready", "w_extra_onehots", "w_extra_picked"))
            landed = 16 * K if gathered else 16

            def row(c, k):
                return msg[:, c, k, :] if gathered else rec[:, c, k, 0:D]

            with nc.Block() as block:
                @block.vector
                def _(dve):
                    n = Count(dve, s_dve)
                    if not gathered:
                        n.link(dve.memset(acc, 0.0))
                        n.link(dve.tensor_scalar(cnt[:, :, :], cnt[:, :, :], 1.0, None, ALU.max))
                        n.link(dve.reciprocal(cnt[:, :, :], cnt[:, :, :]))

                    def onehots(o, r, i, c, k):
                        if gathered:
                            return dve.tensor_scalar(o, iota_r[:, :], r, w_c[:, bass.ds(i * TPI + c * K + k, 1)],
                                                     ALU.is_equal, ALU.mult)
                        return dve.tensor_scalar(o, iota_r[:, :], r, None, ALU.is_equal)

                    def add(i, c, lo):
                        q = i * C + c
                        dve.wait_ge(s_sum, q + 1)
                        wait(dve, s_add, q)
                        dve.tensor_tensor(tile(acc, lo), tile(acc, lo), pY[c % 2][:, 0:D], ALU.add
                                          ).then_inc(s_add, 1)

                    def body(i):
                        los = []
                        for c in range(C):
                            q, b = i * C + c, c % 2
                            lo, hi = span(dve, rows, i, c)
                            los.append(lo)
                            key = cols(dst_c, i, c) if gathered else rec[:, c, :, D:REC].rearrange(
                                "p k a -> p (k a)")
                            if weigh:
                                dve.wait_ge(s_bc, q + 1)

                                def extra_w(t, step):
                                    dve.tensor_scalar(ohTx[:, :], pB[:, :], iota_p[:, bass.ds(t, 1)], None,
                                                      ALU.is_equal).then_inc(s_wxoh, 1)
                                    dve.wait_ge(s_wxmm, step + 1)
                                    dve.sem_inc(s_dve_turn, 1)

                                dve.sem_inc(s_dve_turn, 1)
                                extras(dve, rows, i, c, lo, hi, extra_w)
                                wait(dve, s_wps, q - 1)
                                dve.tensor_scalar(ohT[:, b, :], pB[:, :], iota_p[:, bass.ds(lo, 1)], None,
                                                  ALU.is_equal).then_inc(s_ohT, 1)
                                if c > 0:
                                    add(i, c - 1, los[c - 1])
                                n.link(dve.tensor_tensor(ohR[:, b], *onehot_of(iota_b, cols(et_c, i, c), RELS),
                                                         ALU.is_equal))
                                dve.wait_ge(s_wps, q + 1)
                                n.link(dve.tensor_tensor(
                                    wprod[:, :, :], pC[:, 0:K * RELS].rearrange("p (k r) -> p k r", k=K),
                                    ohR[:, b], ALU.mult))
                                dve.tensor_reduce(cols(w_c, i, c), wprod[:, :, :], AX.X, ALU.add
                                                  ).then_inc(s_wok, 1)
                                dve.wait_ge(s_wok, q + 1)
                            if not gathered:
                                dve.wait_ge(s_in[c], landed * (i + 1))

                            def extra(t, step):
                                dve.tensor_scalar(relx[:, :], key, off[:, bass.ds(t, 1)], None, ALU.subtract
                                                  ).then_inc(s_xrel, 1)
                                dve.wait_ge(s_xrel, step + 1)
                                for k in range(K):
                                    last = onehots(ohNx[:, k, :], relx[:, k:k + 1], i, c, k)
                                last.then_inc(s_xoh, 1)
                                dve.wait_ge(s_xmm, step + 1)
                                wait(dve, s_add, q if weigh or c == 0 else q - 1)
                                dve.tensor_tensor(tile(acc, t), tile(acc, t), pX[:, 0:D], ALU.add
                                                  ).then_inc(s_xadd, 1)
                                dve.wait_ge(s_xadd, step + 1)
                                dve.sem_inc(s_dve_turn, 1)

                            dve.sem_inc(s_dve_turn, 1)
                            extras(dve, rows, i, c, lo, hi, extra)
                            wait(dve, s_sum, q - 1)
                            n.link(dve.tensor_scalar(rel[:, b, :], key, off[:, bass.ds(lo, 1)], None,
                                                     ALU.subtract))
                            for k in range(K):
                                last = onehots(ohN[:, b, k, :], rel[:, b, k:k + 1], i, c, k)
                            last.then_inc(s_oh, 1)
                            if c > 0 and not weigh:
                                add(i, c - 1, los[c - 1])
                        add(i, C - 1, los[C - 1])

                    loop(dve, IT, body, n)

                @block.tensor
                def _(pe):
                    def body(i):
                        if weigh:
                            spread_dst(pe, i, 0, s_ohT, i * C, s_bc)
                        for c in range(C):
                            q, b = i * C + c, c % 2
                            lo, hi = span(pe, rows, i, c)
                            if weigh:
                                wait(pe, s_wok, q)
                                pe.matmul(pC[:, 0:K * RELS], zeros_b[:, 0:P], zeros_b[:, 0:K * RELS],
                                          start=True, stop=False, skip_group_check=True)

                                def extra_w(t, step):
                                    pe.wait_ge(s_wxoh, step + 1)
                                    for k in range(K):
                                        last = pe.matmul(pC[:, k * RELS:(k + 1) * RELS],
                                                         ohTx[:, k * P:(k + 1) * P], tile(cnt, t),
                                                         start=False, stop=False, skip_group_check=True)
                                    last.then_inc(s_wxmm, 1)

                                extras(pe, rows, i, c, lo, hi, extra_w)
                                pe.wait_ge(s_ohT, q + 1)
                                for k in range(K):
                                    last = pe.matmul(pC[:, k * RELS:(k + 1) * RELS],
                                                     ohT[:, b, k * P:(k + 1) * P], tile(cnt, lo),
                                                     start=False, stop=True, skip_group_check=True)
                                last.then_inc(s_wps, 1)
                                if c < C - 1:
                                    spread_dst(pe, i, c + 1, s_ohT, q + 1, s_bc)
                            pe.wait_ge(s_in[c], landed * (i + 1))

                            def extra(t, step):
                                pe.wait_ge(s_xoh, step + 1)
                                for k in range(K):
                                    last = pe.matmul(pX[:, 0:D], ohNx[:, k, :], row(c, k),
                                                     start=k == 0, stop=k == K - 1)
                                last.then_inc(s_xmm, 1)

                            extras(pe, rows, i, c, lo, hi, extra)
                            wait(pe, s_add, q - 1)
                            pe.wait_ge(s_oh, q + 1)
                            for k in range(K):
                                last = pe.matmul(pY[b][:, 0:D], ohN[:, b, k, :], row(c, k),
                                                 start=k == 0, stop=k == K - 1)
                            last.then_inc(s_sum, 1)

                    loop(pe, IT, body)

                if gathered:
                    @block.scalar
                    def _(act):
                        def body(i):
                            for c in range(C):
                                wait(act, s_sum, i * C + c - C + 1)
                                act.sem_inc(s_act_turn, 1)
                                act.copy(slot_u[:, c, :], cols(idx_c, i, c)).then_inc(s_slot, 1)

                        loop(act, IT, body)

                    @block.gpsimd
                    def _(pool):
                        def body(i):
                            for c in range(C):
                                pool.wait_ge(s_slot, i * C + c + 1)
                                pool.sem_inc(s_pool_turn, 1)
                                for k in range(K):
                                    pool.indirect_dma_start(
                                        msg[:, c, k, :], None, table[:, :],
                                        bass.IndirectOffsetOnAxis(ap=slot_u[:, c, k:k + 1], axis=0)
                                    ).then_inc(s_in[c], 16)

                        loop(pool, IT, body)
                else:
                    @block.sync
                    def _(sp):
                        quads = perm[:, :].rearrange("(q p k) f -> q p (k f)", p=P, k=K)

                        def body(i):
                            for c in range(C):
                                wait(sp, s_sum, i * C + c - C + 1)
                                sp.dma_start(rec[:, c, :, :].rearrange("p k f -> p (k f)"),
                                             quads[bass.ds(i * C + c, 1), :, :].rearrange("a p f -> (a p) f")
                                             ).then_inc(s_in[c], 16)

                        sp.dma_start(xy[:, 0:NT - 1, :], x[0:(NT - 1) * P, :].rearrange("(t p) f -> p t f", p=P)
                                     ).then_inc(s_x, 16)
                        sp.dma_start(xy[0:TAIL, NT - 1, :], x[(NT - 1) * P:N, :]).then_inc(s_x, 16)
                        loop(sp, IT, body)
                        sp.wait_ge(s_x, 64)

        def row_stats(name, combine):
            s_d, s_v, s_r = sem(f"{name}_dve"), sem(f"{name}_var"), sem(f"{name}_root")

            @nc_block[0].vector
            def _(dve):
                n = Count(dve, s_d)

                def body(g):
                    for k in range(XT):
                        last = combine(dve, g * XT + k)
                    n.link(last)
                    for k in range(XT):
                        last = dve.bn_stats(stats[:, bass.ds(g * XT + k, 1), :].rearrange("p a s -> p (a s)"),
                                            tile(xy, g * XT + k))
                    n.link(last)

                loop(dve, HG, body, n)
                n.link(dve.tensor_tensor(mean[:, :], stats[:, :, 1], stats[:, :, 4], ALU.add))
                n.link(dve.tensor_tensor(half[:, :], stats[:, :, 1], stats[:, :, 4], ALU.subtract))
                n.link(dve.tensor_tensor(rstd[:, :], stats[:, :, 2], stats[:, :, 5], ALU.add))
                n.link(dve.tensor_tensor(half[:, :], half[:, :], half[:, :], ALU.mult))
                n.link(dve.tensor_scalar(mean[:, :], mean[:, :], 0.5, None, ALU.mult))
                n.link(dve.tensor_scalar(rstd[:, :], rstd[:, :], 1.0 / D, None, ALU.mult))
                n.link(dve.scalar_tensor_tensor(out=rstd[:, :], in0=half[:, :], scalar=0.25, in1=rstd[:, :],
                                                op0=ALU.mult, op1=ALU.add))
                dve.sem_inc(s_v, 1)
                dve.wait_ge(s_r, 1)
                n.link(dve.reciprocal(rstd[:, :], rstd[:, :]))

                def normalise(g):
                    for k in range(XT):
                        t = g * XT + k
                        last = dve.tensor_scalar(tile(xy, t), tile(xy, t), mean[:, bass.ds(t, 1)],
                                                 rstd[:, bass.ds(t, 1)], ALU.subtract, ALU.mult)
                    last.then_inc(s_norm[0], 1)

                loop(dve, HG, normalise)

            @nc_block[0].scalar
            def _(act):
                act.wait_ge(s_v, 1)
                act.activation(rstd[:, :], rstd[:, :], ACT.Sqrt, bias=eps_t[:, 0:1]).then_inc(s_r, 1)

        nc_block, s_norm = [None], [None]

        def make_table(name, layer):
            s_hs, s_ht, s_htc, s_mm, s_dve, s_sd, s_sa = (sem(f"{name}_{n}") for n in (
                "h_ready", "h_transposed", "hT_copied", "products", "acc_set", "stage_dve", "stage_act"))
            s_out = [sem(f"{name}_stored{b}") for b in range(2)]
            s_wl = sem(f"{name}_weights_in")
            M0, M1, M2 = (pB, pR), (pY0, pY1), (pC, pX)

            with nc.Block() as block:
                @block.scalar
                def _(act):
                    def body(j):
                        for b in range(2):
                            t = 2 * j + b
                            wait(act, s_ht, t - 1)
                            act.sem_inc(s_act_turn, 1)
                            if layer == 0:
                                act.copy(hs[:, b, :], tile(xy, t)).then_inc(s_hs, 1)
                            else:
                                act.activation(hs[:, b, :], tile(acc, t), ACT.Relu).then_inc(s_hs, 1)
                        for b in range(2):
                            t = 2 * j + b
                            act.wait_ge(s_ht, t + 1)
                            wait(act, s_mm, 3 * (t - 1))
                            act.copy(hT[:, b, :], pT[b][:, 0:P]).then_inc(s_htc, 1)
                        for b in range(2):
                            t = 2 * j + b
                            wait(act, s_out[b], 16 * j)
                            act.wait_ge(s_mm, 3 * t + 1)
                            act.copy(stage[:, b, 0:512], M0[b][:, :]).then_inc(s_sa, 1)

                    loop(act, NT // 2, body)

                @block.vector
                def _(dve):
                    def body(j):
                        for b in range(2):
                            t = 2 * j + b
                            wait(dve, s_out[b], 16 * j)
                            dve.wait_ge(s_mm, 3 * t + 2)
                            dve.tensor_copy(stage[:, b, 512:MAIN], M1[b][:, :]).then_inc(s_sd, 1)
                            dve.wait_ge(s_mm, 3 * t + 3)
                            dve.tensor_tensor(tile(acc, t), M2[b][:, 0:D], bias_all[:, layer, :], ALU.add
                                              ).then_inc(s_dve, 1)

                    loop(dve, NT // 2, body)

                @block.tensor
                def _(pe):
                    def body(j):
                        for b in range(2):
                            t = 2 * j + b
                            pe.wait_ge(s_hs, t + 1)
                            wait(pe, s_htc, t - 1)
                            pe.transpose(pT[b][:, 0:P], hs[:, b, :], ident[:, :]).then_inc(s_ht, 1)
                        for b in range(2):
                            t = 2 * j + b
                            pe.wait_ge(s_htc, t + 1)
                            wait(pe, s_sa, t - 1)
                            pe.matmul(M0[b][:, :], hT[:, b, :], w_all[:, 0:512], start=True, stop=True
                                      ).then_inc(s_mm, 1)
                            wait(pe, s_sd, t - 1)
                            pe.matmul(M1[b][:, :], hT[:, b, :], w_all[:, 512:MAIN], start=True, stop=True
                                      ).then_inc(s_mm, 1)
                            wait(pe, s_dve, t - 1)
                            pe.matmul(M2[b][:, 0:D], hT[:, b, :], w_all[:, MAIN:MAIN + D], start=True, stop=True
                                      ).then_inc(s_mm, 1)

                    if layer:
                        pe.wait_ge(s_wl, 32)
                    loop(pe, NT // 2, body)

                @block.sync
                def _(sp):
                    if layer:
                        sp.dma_start(w_all[:, 0:MAIN].rearrange("p (r o) -> p r o", r=RELS),
                                     weights[layer].rearrange("r i o -> i r o")).then_inc(s_wl, 16)
                        sp.dma_start(w_all[:, MAIN:MAIN + D], roots[layer]).then_inc(s_wl, 16)
                    tiles = table[:, :].rearrange("(r t p) f -> t p r f", r=RELS, p=P)

                    def body(j):
                        for b in range(2):
                            t = 2 * j + b
                            sp.wait_ge(s_sa, t + 1)
                            sp.wait_ge(s_sd, t + 1)
                            sp.dma_start(tiles[bass.ds(t, 1)].rearrange("a p r f -> (a p) r f"),
                                         stage[:, b, :].rearrange("p (r f) -> p r f", r=RELS)
                                         ).then_inc(s_out[b], 16)

                    loop(sp, NT // 2, body)
                    for b in range(2):
                        sp.wait_ge(s_out[b], 16 * (NT // 2))

        reduce_pass("gcn", row_s, gathered=False, weigh=False)

        with nc.Block() as block:
            nc_block[0], s_norm[0] = block, sem("x1_ready")
            row_stats("ln1", lambda dve, t: dve.scalar_tensor_tensor(
                out=tile(xy, t), in0=tile(acc, t), scalar=dis[:, bass.ds(t, 1)], in1=tile(xy, t),
                op0=ALU.mult, op1=ALU.add))

        make_table("table1", 0)
        reduce_pass("rgcn1", row_n, gathered=True, weigh=True)
        make_table("table2", 1)
        reduce_pass("rgcn2", row_n, gathered=True, weigh=False)

        s_o = sem("out_stored")
        with nc.Block() as block:
            nc_block[0], s_norm[0] = block, sem("out_ready")
            row_stats("ln2", lambda dve, t: dve.tensor_tensor(tile(xy, t), tile(xy, t), tile(acc, t), ALU.add))

            @block.sync
            def _(sp):
                groups = out[0:(HG - 1) * XT * P, :].rearrange("(g t p) f -> g p t f", t=XT, p=P)

                def body(g):
                    sp.wait_ge(s_norm[0], g + 1)
                    sp.dma_start(groups[bass.ds(g, 1)].rearrange("a p t f -> (a p) t f"),
                                 xy[:, bass.ds(g * XT, XT), :]).then_inc(s_o, 16)

                loop(sp, HG - 1, body)
                sp.wait_ge(s_norm[0], HG)
                t0 = (HG - 1) * XT
                sp.dma_start(out[t0 * P:(NT - 1) * P, :].rearrange("(t p) f -> p t f", p=P),
                             xy[:, t0:NT - 1, :]).then_inc(s_o, 16)
                sp.dma_start(out[(NT - 1) * P:N, :], xy[0:TAIL, NT - 1, :]).then_inc(s_o, 16)
                sp.wait_ge(s_o, 16 * (HG + 1))


INS = ["x", "src", "dst", "edge_type_8", "L0_gnn_W", "L0_gnn_b", "L1_gnn_weights", "L1_gnn_roots",
       "L1_gnn_biases"]


def kernel(**inputs):
    import concourse.bacc as bacc
    from concourse.bass_utils import run_bass_kernel_spmd

    nc = bacc.Bacc("TRN2", target_bir_lowering=False, num_devices=1)
    arrays, args = {}, []
    for name in INS:
        a = np.ascontiguousarray(inputs[name])
        arrays[f"in_{name}"] = a
        args.append(nc.dram_tensor(f"in_{name}", a.shape, mybir.dt.from_np(a.dtype), kind="ExternalInput").ap())
    out = nc.dram_tensor("out_0", inputs["x"].shape, F32, kind="ExternalOutput").ap()
    build(nc, *args, out)
    r = run_bass_kernel_spmd(nc, [arrays], core_ids=[0])
    return r.results[0]["out_0"]
```
